# Optimizing a Trainium2 kernel written in Bass

```python
import numpy as np
import jax
import jax.numpy as jnp

def _softmax(x, axis=-1):
    return jax.nn.softmax(x, axis=axis)

def _gelu(x):
    return jax.nn.gelu(x, approximate=True)

def _silu(x):
    return jax.nn.silu(x)

def _sigmoid(x):
    return jax.nn.sigmoid(x)

def _layernorm(x, axis=-1, eps=1e-05):
    m = jnp.mean(x, axis=axis, keepdims=True)
    v = jnp.var(x, axis=axis, keepdims=True)
    return (x - m) / jnp.sqrt(v + eps)

def _scatter_add(tgt, idx, src, axis=0):
    return tgt.at[idx].add(src)

def _segment_sum(src, seg, n):
    return jax.ops.segment_sum(src, seg, n)
kernel_name = 'mk_audio_tower_d1_tok_audfeat1024_r4_675259'

def setup_inputs(seed: int=0):
    np.random.seed(seed)
    _w = jnp.asarray

    def _rec_inputs():
        import jax
        import jax.numpy as jnp
        _rk = jax.random.key(seed)
        x = -0.000124254 + 0.999853 * jax.random.normal(jax.random.fold_in(_rk, 1), (8, 750, 256), jnp.float32)
        return x
    x = _rec_inputs()

    def _L0_tok_setup():
        import jax, jax.numpy as jnp
        import numpy as np
        CONTEXT = (-3, 0, 3)
        SUBSAMPLING = 1
        FEAT_DIM = 256
        OUT_DIM = 256
        key = jax.random.key(seed)
        k1, k2, k3 = jax.random.split(key, 3)
        mb, t = (32, 250)
        x = jax.random.normal(k1, (mb, t, FEAT_DIM), dtype=jnp.float32)
        in_dim = FEAT_DIM * len(CONTEXT)
        scale = 1.0 / np.sqrt(in_dim)
        W = jax.random.uniform(k2, (OUT_DIM, in_dim), dtype=jnp.float32, minval=-scale, maxval=scale)
        b = jax.random.uniform(k3, (OUT_DIM,), dtype=jnp.float32, minval=-scale, maxval=scale)
        return {'input': x, 'W': W, 'b': b}
    _L0_tok_all = _L0_tok_setup()
    _L0_tok_in = {k: v for k, v in _L0_tok_all.items() if k in ('W', 'b')}
    del _L0_tok_all

    def _L0_attn_setup():
        import math
        import jax, jax.numpy as jnp
        import numpy as np
        N_EMBD = 256
        N_HEAD = 16
        key = jax.random.key(seed)
        ks = jax.random.split(key, 6)
        C = N_EMBD
        scale = 1.0 / math.sqrt(C)
        x = jax.random.normal(ks[0], (2, 512, C), dtype=jnp.float32)
        Wk = jax.random.normal(ks[1], (C, C), dtype=jnp.float32) * scale
        Wq = jax.random.normal(ks[2], (C, C), dtype=jnp.float32) * scale
        Wv = jax.random.normal(ks[3], (C, C), dtype=jnp.float32) * scale
        Wp = jax.random.normal(ks[4], (C, C), dtype=jnp.float32) * scale
        bp = jax.random.normal(ks[5], (C,), dtype=jnp.float32) * scale
        return {'x': x, 'Wk': Wk, 'Wq': Wq, 'Wv': Wv, 'Wp': Wp, 'bp': bp}
    _L0_attn_all = _L0_attn_setup()
    _L0_attn_in = {k: v for k, v in _L0_attn_all.items() if k in ('Wk', 'Wq', 'Wv', 'Wp', 'bp')}
    del _L0_attn_all

    def _L0_ffn_setup():
        import jax, jax.numpy as jnp
        import numpy as np
        B, S, D, H, E, K = (4, 512, 256, 1024, 4, 2)
        key = jax.random.key(seed)
        ks = jax.random.split(key, 7)
        s1 = 1.0 / np.sqrt(D)
        s2 = 1.0 / np.sqrt(H)
        return {'x': jax.random.normal(ks[0], (B, S, D), jnp.float32), 'w1': jax.random.uniform(ks[1], (E, D, H), jnp.float32, -s1, s1), 'b1': jax.random.uniform(ks[2], (E, H), jnp.float32, -s1, s1), 'w2': jax.random.uniform(ks[3], (E, H, D), jnp.float32, -s2, s2), 'b2': jax.random.uniform(ks[4], (E, D), jnp.float32, -s2, s2), 'wr': jax.random.uniform(ks[5], (D, E), jnp.float32, -s1, s1), 'br': jax.random.uniform(ks[6], (E,), jnp.float32, -s1, s1)}
    _L0_ffn_all = _L0_ffn_setup()
    _L0_ffn_in = {k: v for k, v in _L0_ffn_all.items() if k in ('w1', 'b1', 'w2', 'b2', 'wr', 'br')}
    del _L0_ffn_all
    return {'x': x, 'L0_tok_W': _L0_tok_in['W'], 'L0_tok_b': _L0_tok_in['b'], 'L0_attn_Wk': _L0_attn_in['Wk'], 'L0_attn_Wq': _L0_attn_in['Wq'], 'L0_attn_Wv': _L0_attn_in['Wv'], 'L0_attn_Wp': _L0_attn_in['Wp'], 'L0_attn_bp': _L0_attn_in['bp'], 'L0_ffn_w1': _L0_ffn_in['w1'], 'L0_ffn_b1': _L0_ffn_in['b1'], 'L0_ffn_w2': _L0_ffn_in['w2'], 'L0_ffn_b2': _L0_ffn_in['b2'], 'L0_ffn_wr': _L0_ffn_in['wr'], 'L0_ffn_br': _L0_ffn_in['br']}

def reference(x, L0_tok_W, L0_tok_b, L0_attn_Wk, L0_attn_Wq, L0_attn_Wv, L0_attn_Wp, L0_attn_bp, L0_ffn_w1, L0_ffn_b1, L0_ffn_w2, L0_ffn_b2, L0_ffn_wr, L0_ffn_br):
    import jax
    import jax.numpy as jnp

    def _L0_tok_ref(input, W, b):
        import jax, jax.numpy as jnp
        import numpy as np
        CONTEXT = (-3, 0, 3)
        SUBSAMPLING = 1
        FEAT_DIM = 256
        OUT_DIM = 256
        mb, t, d = input.shape
        offsets = [c - CONTEXT[0] for c in CONTEXT]
        width = CONTEXT[-1] - CONTEXT[0]
        t_out = (t - width - 1) // SUBSAMPLING + 1
        x = jnp.concatenate([input[:, o:o + (t_out - 1) * SUBSAMPLING + 1:SUBSAMPLING, :] for o in offsets], axis=-1)
        return jnp.einsum('btd,od->bto', x, W) + b

    def _L0_attn_ref(x, Wk, Wq, Wv, Wp, bp):
        import math
        import jax, jax.numpy as jnp
        import numpy as np
        N_EMBD = 256
        N_HEAD = 16
        B, T, C = x.shape
        H = N_HEAD
        D = C // H

        def heads(W):
            return (x @ W.T).reshape(B, T, H, D).transpose(0, 2, 1, 3)
        k = heads(Wk)
        q = heads(Wq)
        v = heads(Wv)
        att = jnp.einsum('bhqd,bhkd->bhqk', q, k) / math.sqrt(D)
        causal = jnp.tril(jnp.ones((T, T), dtype=bool))
        att = jnp.where(causal, att, -jnp.inf)
        att = jax.nn.softmax(att, axis=-1)
        y = jnp.einsum('bhqk,bhkd->bhqd', att, v)
        y = y.transpose(0, 2, 1, 3).reshape(B, T, C)
        return y @ Wp.T + bp

    def _L0_ffn_ref(x, w1, b1, w2, b2, wr, br):
        import jax, jax.numpy as jnp
        import numpy as np
        B, S, D, H, E, K = (4, 512, 256, 1024, 4, 2)
        Bx, Sx, Dx = x.shape
        xf = x.reshape(-1, Dx)
        logits = xf @ wr + br
        topk_vals, topk_idx = jax.lax.top_k(logits, K)
        gates = jax.nn.softmax(topk_vals, axis=-1)
        h = jax.nn.gelu(jnp.einsum('nd,edh->enh', xf, w1) + b1[:, None, :], approximate=False)
        y = jnp.einsum('enh,ehd->end', h, w2) + b2[:, None, :]
        c = jnp.einsum('eh,ehd->ed', jax.nn.gelu(b1, approximate=False), w2) + b2
        c_sum = c.sum(axis=0)
        yt = jnp.transpose(y, (1, 0, 2))
        y_sel = jnp.take_along_axis(yt, topk_idx[:, :, None], axis=1)
        c_sel = c[topk_idx]
        out = jnp.einsum('nk,nkd->nd', gates, y_sel - c_sel + c_sum[None, None, :])
        return out.reshape(Bx, Sx, Dx)
    h = _L0_tok_ref(x, L0_tok_W, L0_tok_b)
    h = h + _L0_attn_ref(_layernorm(h, axis=-1), L0_attn_Wk, L0_attn_Wq, L0_attn_Wv, L0_attn_Wp, L0_attn_bp)
    h = h + _L0_ffn_ref(_layernorm(h, axis=-1), L0_ffn_w1, L0_ffn_b1, L0_ffn_w2, L0_ffn_b2, L0_ffn_wr, L0_ffn_br)
    return h

_drawn_inputs = setup_inputs


def setup_inputs(seed=0):
    import zlib

    import numpy as np

    out = dict(_drawn_inputs(seed))
    spreads = {}
    factors = {}
    for name, (base, spread) in spreads.items():
        noise = np.random.default_rng([zlib.crc32(name.encode()), seed]).standard_normal(out[name].shape)
        drawn = base * np.exp(spread * noise) if base else spread * noise
        out[name] = jnp.asarray(drawn.astype(out[name].dtype))
    for name, factor in factors.items():
        out[name] = (out[name] * factor).astype(out[name].dtype)
    return out
```

```python
import numpy as np
import concourse.bass as bass
import concourse.mybir as mybir
from contextlib import ExitStack

fp32, fp32r, bf16 = mybir.dt.float32, mybir.dt.float32r, mybir.dt.bfloat16
ALU = mybir.AluOpType
ACT = mybir.ActivationFunctionType
AX = mybir.AxisListType

NB, T_IN, D = 8, 750, 256
SHIFTS = (0, 3, 6)
T = T_IN - SHIFTS[-1]
NT = 6
TT = T // NT
HALF = T // 2
NH, DH = 16, 16
NG, HG = 4, 4
KC = D // 128
EPS = 1e-5
NEG = -1.0e30
assert TT * NT == T and TT <= 128 and HALF <= 512

K_PARTS = (0, 0, 0, 1, 1, 2)
Q_PARTS = (0, 1, 2, 0, 1, 0)
ROWS = DH * len(K_PARTS)
NPART = 3

MX = ([(5, h, 1, s * HALF, HALF) for h in range(HG) for s in range(2)]
      + [(4, h, 1, s * 310, 310) for h in range(HG) for s in range(2)]
      + [(i, h, 1, 0, (i + 1) * TT) for i in (3, 2) for h in range(HG)]
      + [(1, h, 2, 0, 2 * TT) for h in (0, 2)]
      + [(0, 0, 4, 0, TT)])
ST = ([[(0, h, s * HALF, HALF)] for h in range(HG) for s in range(2)]
      + [[(1, h, TT + s * 310, 310)] for h in range(HG) for s in range(2)]
      + [[(2, h, 2 * TT, 4 * TT)] for h in range(HG)]
      + [[(3, h, 3 * TT, 3 * TT), (5, h, 5 * TT, TT)] for h in range(HG)]
      + [[(4, h, 4 * TT, 2 * TT), (4, h + 1, 4 * TT, 2 * TT)] for h in (0, 2)])
NMX, NST = len(MX), len(ST)
MXB, STB = 3, 2
assert (NG * NMX) % MXB == 0 and (NG * NST) % STB == 0
PV_ORDER = (0, 1, 2, 3, 5, 4)
PV_AFTER = (8, 16, 20, 24, 24, 26)
LEAD = 12


def later(value):
    return not isinstance(value, int) or value > 0


def wait_apart(eng, sem, value, apart):
    eng.wait_ge(sem, value)
    if not isinstance(value, int):
        eng.sem_inc(apart, 1)


def mx_events(first, last):
    for u in range(first, last):
        yield "mx", u
        g, k = divmod(u, NMX)
        if g and k in (1, 3, 4):
            yield {1: "mx_row", 3: "mx_turn", 4: "mx_neg"}[k], g - 1


def front_events():
    yield "x", 0
    for i in range(NT):
        yield "tok", i
    yield "norm_scale", 0
    for n in range(4):
        yield "turn", n
    for m in range(KC):
        for n in range(4):
            yield "qk", 4 * m + n
        yield "load_stack", 2 * m
        yield "load_stack", 2 * m + 1
    yield from mx_events(0, NMX + LEAD)


def body_events(first, last):
    beside = {}

    def put(s, *event):
        beside.setdefault(s, []).append(event)

    for i in range(NT):
        put(i, "v", i)
        if not first:
            put(7 + 3 * i, "proj", i)
        if not last:
            put(24 + 3 * i, "tok", i)
    if not first:
        put(23, "h2_store", 0)
    put(30, "res_load", 0)
    if not last:
        put(6, "x", 0)
        put(40, "norm_scale", 0)
        for n in range(4):
            put(48 + n, "turn", n)
            put(53 + 2 * n, "qk", n)
            put(66 + 4 * n, "qk", n + 4)
        put(60, "load_stack", 0)
        put(60, "load_stack", 1)
        put(81, "load_stack", 2)
        put(NG * NST - 1, "load_stack", 3)
    else:
        for s, kind in ((68, "mx_row"), (70, "mx_turn"), (72, "mx_neg")):
            put(s, kind, NG - 1)
    mx_at = NMX + LEAD
    mx_end = NG * NMX if last else NG * NMX + NMX + LEAD
    for s in range(NG * NST):
        want = min(NMX + LEAD + (s + 1) * NMX // NST, mx_end)
        yield from mx_events(mx_at, want)
        mx_at = max(mx_at, want)
        g, k = divmod(s, NST)
        yield "st", s
        yield from beside.get(s, ())
        for o in range(NT - 1):
            if PV_AFTER[o] + 1 == k:
                yield "pv", (g, o)
        if g and k == 1:
            yield "pv", (g - 1, NT - 1)
        if g and k == 4:
            yield "attn_norm", g - 1
    yield "pv", (NG - 1, NT - 1)
    yield "attn_norm", NG - 1


def bank_in_turn(events):
    held, turning = [], False
    for e in events:
        if turning and e[0] in ("v", "proj", "tok", "turn", "qk", "norm_scale", "load_stack", "h2_store"):
            held.append(e)
            continue
        yield e
        if e[0] == "mx_turn":
            turning = True
        if e[0] == "mx_neg":
            turning = False
            yield from held
            held = []


def tail_events():
    for i in range(NT):
        yield "proj", i
    yield "h2_store", 0


def over_batches(eng, emit):
    emit(front_events(), 0, 0)
    emit(bank_in_turn(body_events(True, False)), 0, 1)
    with eng.Fori(1, NB - 1) as b:
        emit(bank_in_turn(body_events(False, False)), b, b + 1)
    emit(bank_in_turn(body_events(False, True)), NB - 1, NB)
    emit(tail_events(), NB, NB + 1)


def attention_phase(nc, xT, tokWT, tokb, wkT, wqT, wvT, wpT, bp, h1_s, qk_s, h2_s):
    with ExitStack() as es:
        def sb(name, shape, dt=fp32):
            return es.enter_context(nc.sbuf_tensor(name, shape, dt))

        def ps(name, shape):
            return es.enter_context(nc.psum_tensor(name, shape, fp32))

        def sem(name):
            return es.enter_context(nc.semaphore(name))

        tokw = [sb(f"tokw{p}", [128, 3 * KC, D], fp32r) for p in range(2)]
        qkvw = [sb(f"qkvw{p}", [128, 3 * KC, D], fp32r) for p in range(2)]
        projw = sb("projw", [128, NG, D])
        tokb_row = sb("tokb_row", [TT, D])
        bp_row = sb("bp_row", [TT, D])
        ident = sb("ident", [128, 128])
        identb = sb("identb", [TT, TT], bf16)
        mask_qk = sb("mask_qk", [TT, TT], bf16)
        mask_kq = sb("mask_kq", [TT, TT], bf16)
        power = sb("power", [TT, NT])
        xraw = sb("xraw", [128, T_IN])
        xp = [sb(f"xp{p}", [128, KC, T_IN], fp32r) for p in range(2)]
        h1 = sb("h1", [TT, NT, D])
        stats = sb("stats", [TT, NT, 6])
        mv = sb("mv", [TT, NT, 2])
        veps = sb("veps", [TT, NT])
        rstd = sb("rstd", [TT, NT])
        xn = sb("xn", [TT, NT, D])
        xnT = [sb(f"xnT{p}", [128, KC, T], fp32r) for p in range(2)]
        parts = sb("parts", [128, 2, NPART, HALF], bf16)
        rest = sb("rest", [128, 2, HALF])
        kst = [sb(f"kst{g}", [ROWS + NPART, HG, T], bf16) for g in range(NG)]
        qst = [sb(f"qst{g}", [ROWS + NPART, HG, T], bf16) for g in range(NG)]
        vaug = sb("vaug", [TT, NT, NH, 2 * DH])
        mxp = sb("mxp", [TT, 2, HG * NT, 2])
        mxg = sb("mxg", [TT, HG * NT])
        negm = sb("negm", [HG * NT, TT])
        negr = sb("negr", [HG * NT, TT])
        negp = sb("negp", [HG * NT, NPART, TT], bf16)
        prob = {0: sb("prob0", [128, HG, T]), 1: sb("prob1", [128, HG, T - TT]),
                2: sb("prob2", [TT, HG, 4 * TT]), 4: sb("prob4", [TT, HG, 2 * TT])}
        prob35 = sb("prob35", [TT, HG, 4 * TT])
        sums = sb("sums", [128, T])
        onT = sb("onT", [128, NG, T])
        res = sb("res", [TT, NT, D])

        mxb = [ps(f"mxb{i}", [128, 512]) for i in range(MXB)]
        stb = [ps(f"stb{i}", [128, 512]) for i in range(STB)]
        pvb = ps("pvb", [128, 2, 512])
        pab = ps("pab", [128, 512])

        def sem(name):
            return es.enter_context(nc.semaphore(name))

        w_loaded, w_top, w_split = sem("w_loaded"), sem("w_top"), sem("w_split")
        rows_loaded, zeroed, consts = sem("rows_loaded"), sem("zeroed"), sem("consts")
        x_loaded, x_top, x_split = sem("x_loaded"), sem("x_top"), sem("x_split")
        tok_full, tok_evac, bn_done, aggr_done = sem("tok_full"), sem("tok_evac"), sem("bn_done"), sem("aggr_done")
        veps_ready, rstd_ready, xn_ready = sem("veps_ready"), sem("rstd_ready"), sem("xn_ready")
        h1_bias, h1_stored = sem("h1_bias"), sem("h1_stored")
        turn_full, turn_top, turn_evac = sem("turn_full"), sem("turn_top"), sem("turn_evac")
        qk_full, qk_top, qk_evac = sem("qk_full"), sem("qk_top"), sem("qk_evac")
        qk_mid, qk_low = sem("qk_mid"), sem("qk_low")
        parts_stored = [sem(f"parts_stored{i}") for i in range(2)]
        stack_loaded = [sem(f"stack_loaded{g}") for g in range(NG)]
        mx_full, mx_red, row_max = sem("mx_full"), sem("mx_red"), sem("row_max")
        max_full, max_evac, neg_split, negm_loaded = sem("max_full"), sem("max_evac"), sem("neg_split"), sem("negm_loaded")
        st_full, exp_done, pv_full = sem("st_full"), sem("exp_done"), sem("pv_full")
        sums_moved, sums_inv, attn_evac = sem("sums_moved"), sem("sums_inv"), sem("attn_evac")
        v_full, v_evac = sem("v_full"), sem("v_evac")
        proj_full, proj_evac, res_loaded, h2_stored = sem("proj_full"), sem("proj_evac"), sem("res_loaded"), sem("h2_stored")
        apart = {e: sem(f"apart_{e}") for e in ("sp", "pool", "dve")}
        block = es.enter_context(nc.Block())

        tok_stage = prob[0][:, :, :].rearrange("p h t -> p (h t)")[:, 0:3 * KC * D].rearrange("p (c d) -> p c d", d=D)
        qkv_stage = prob[1][:, :, :].rearrange("p h t -> p (h t)")[:, 0:3 * KC * D].rearrange("p (c d) -> p c d", d=D)

        @block.sync
        def _(sp):
            sp.dma_start(tok_stage, tokWT.rearrange("(c p) d -> p c d", p=128)).then_inc(w_loaded, 16)
            for n, w in enumerate((wkT, wqT, wvT)):
                sp.dma_start(qkv_stage[:, KC * n:KC * n + KC, :], w.rearrange("(c p) d -> p c d", p=128)).then_inc(w_loaded, 16)
            sp.dma_start(tokb_row[:, :], tokb.partition_broadcast(TT)).then_inc(rows_loaded, 16)
            sp.dma_start(bp_row[:, :], bp.partition_broadcast(TT)).then_inc(rows_loaded, 16)
            sp.wait_ge(zeroed, 2)
            for h in range(HG):
                sp.dma_start(projw[2 * DH * h:2 * DH * h + DH, :, :],
                             wpT.rearrange("(g h r) d -> h r g d", g=NG, h=HG)[h]).then_inc(rows_loaded, 16)

            def emit(events, b, a):
                for kind, n in events:
                    if kind == "x":
                        for c in range(KC):
                            if later(a * KC + c):
                                wait_apart(sp, x_split, a * KC + c, apart["sp"])
                            sp.dma_start(xraw[:, :], xT[a, 128 * c:128 * c + 128, :]).then_inc(x_loaded, 16)
                    if kind == "norm_scale":
                        wait_apart(sp, h1_bias, a + 1, apart["sp"])
                        sp.dma_start(h1_s[a].rearrange("(i p) d -> p i d", p=TT), h1[:, :, :]).then_inc(h1_stored, 16)
                    if kind == "qk":
                        wait_apart(sp, qk_low, a * 8 + n + 1, apart["sp"])
                        for t in range(NPART):
                            sp.dma_start(qk_s[a, n // 2 % 2, 8 * (n // 4):8 * (n // 4) + 8, t, :,
                                              n % 2 * HALF:(n % 2 + 1) * HALF], parts[:, n % 2, t, :]).then_inc(parts_stored[n % 2], 16)
                    if kind == "load_stack":
                        for i in range(2):
                            wait_apart(sp, parts_stored[i], a * (4 * 16 * NPART) + 2 * 16 * NPART * (n // 2 + 1), apart["sp"])
                        if later(a):
                            wait_apart(sp, st_full, a * (NG * NST) + (n + 1 - NG) * NST, apart["sp"])
                        for at, t in enumerate(K_PARTS):
                            sp.dma_start(kst[n][DH * at:DH * at + DH, :, :],
                                         qk_s[a, 0, HG * n:HG * n + HG, t].rearrange("h r c -> r h c")).then_inc(stack_loaded[n], 16)
                        for at, r in ((0, 3), (3, 2), (5, 1)):
                            sp.dma_start(qst[n][DH * at:DH * (at + r), :, :],
                                         qk_s[a, 1, HG * n:HG * n + HG, 0:r].rearrange("h t r c -> (t r) h c")
                                         ).then_inc(stack_loaded[n], 16)
                    if kind == "mx_neg":
                        wait_apart(sp, neg_split, b * (4 * NG) + 4 * (n + 1), apart["sp"])
                        for t in range(NPART):
                            sp.dma_start(qst[n % NG][ROWS + t:ROWS + t + 1, :, :]
                                         .rearrange("p h (i q) -> p (h i) q", i=NT), negp[:, t, :]).then_inc(negm_loaded, 16)
                    if kind == "res_load":
                        if later(b):
                            wait_apart(sp, h2_stored, b * 16, apart["sp"])
                        wait_apart(sp, h1_stored, b * 16 + 16, apart["sp"])
                        sp.dma_start(res[:, :, :], h1_s[b].rearrange("(i p) d -> p i d", p=TT)).then_inc(res_loaded, 16)
                    if kind == "h2_store":
                        wait_apart(sp, proj_evac, b * NT, apart["sp"])
                        sp.dma_start(h2_s[b - 1].rearrange("(i p) d -> p i d", p=TT), res[:, :, :]).then_inc(h2_stored, 16)

            over_batches(sp, emit)
            wait_apart(sp, h2_stored, NB * 16, apart["sp"])

        @block.gpsimd
        def _(pool):
            pool.memset(projw[:, :, :], 0.0).then_inc(zeroed, 1)
            pool.memset(vaug[:, :, :, :], 1.0).then_inc(zeroed, 1)
            for m, v in ((ident, 0.0), (identb, 0.0), (mask_qk, 0.0), (mask_kq, 0.0), (power, -0.5)):
                pool.memset(m[:, :], v).then_inc(consts, 1)
            pool.wait_ge(consts, 5)
            for m in (ident, identb):
                pool.affine_select(out=m[:, :], in_=m[:, :], compare_op=ALU.not_equal, fill=1.0, base=0,
                                   pattern=[[-1, m.shape[1]]], channel_multiplier=1).then_inc(consts, 1)
            pool.affine_select(out=mask_qk[:, :], in_=mask_qk[:, :], compare_op=ALU.is_ge, fill=NEG, base=0,
                               pattern=[[-1, TT]], channel_multiplier=1).then_inc(consts, 1)
            pool.affine_select(out=mask_kq[:, :], in_=mask_kq[:, :], compare_op=ALU.is_ge, fill=NEG, base=0,
                               pattern=[[1, TT]], channel_multiplier=-1).then_inc(consts, 1)
            pool.wait_ge(consts, 9)
            for g in range(NG):
                if g:
                    pool.wait_ge(consts, 9 + g)
                pool.memset(kst[g][ROWS:ROWS + NPART, :, :], 1.0).then_inc(consts, 1)
            pool.wait_ge(consts, 9 + NG)

            def emit(events, b, a):
                for kind, n in events:
                    if kind == "x":
                        for c in range(KC):
                            wait_apart(pool, x_loaded, a * (16 * KC) + 16 * (c + 1), apart["pool"])
                            if c == 0 and later(a):
                                wait_apart(pool, tok_full, a * NT, apart["pool"])
                            pool.tensor_copy(xp[0][:, c, :], xraw[:, :]).then_inc(x_top, 1)
                            pool.wait_ge(x_top, a * KC + c + 1)
                            pool.tensor_tensor(xp[1][:, c, :], xraw[:, :], xp[0][:, c, :].bitcast(fp32),
                                               ALU.subtract).then_inc(x_split, 1)
                    if kind == "norm_scale":
                        pool.wait_ge(veps_ready, a + 1)
                        pool.tensor_tensor(rstd[:, :], veps[:, :], power[:, :], ALU.pow).then_inc(rstd_ready, 1)
                        pool.wait_ge(xn_ready, a * NT + NT)
                        if isinstance(a, int) and a == 0:
                            pool.wait_ge(rows_loaded, 16 * 6)
                        pool.tensor_tensor(h1[:, :, :], h1[:, :, :],
                                           bp_row[:, :].unsqueeze(1).broadcast_to([TT, NT, D]), ALU.add).then_inc(h1_bias, 1)
                    if kind == "qk":
                        wait_apart(pool, qk_evac, a * 8 + n + 1, apart["pool"])
                        pool.tensor_copy(parts[:, n % 2, 1, :], rest[:, n % 2, :]).then_inc(qk_mid, 1)
                        pool.wait_ge(qk_mid, a * 8 + n + 1)
                        pool.tensor_tensor(parts[:, n % 2, 2, :], rest[:, n % 2, :], parts[:, n % 2, 1, :],
                                           ALU.subtract).then_inc(qk_low, 1)
                    if kind == "mx_neg":
                        wait_apart(pool, max_evac, b * NG + n + 1, apart["pool"])
                        if later(b * NG + n):
                            wait_apart(pool, negm_loaded, b * (48 * NG) + 48 * n, apart["pool"])
                        pool.tensor_copy(negp[:, 0, :], negm[:, :]).then_inc(neg_split, 1)
                        pool.wait_ge(neg_split, b * (4 * NG) + 4 * n + 1)
                        pool.tensor_tensor(negr[:, :], negm[:, :], negp[:, 0, :], ALU.subtract).then_inc(neg_split, 1)
                        wait_apart(pool, neg_split, b * (4 * NG) + 4 * n + 2, apart["pool"])
                        pool.tensor_copy(negp[:, 1, :], negr[:, :]).then_inc(neg_split, 1)
                        pool.wait_ge(neg_split, b * (4 * NG) + 4 * n + 3)
                        pool.tensor_tensor(negp[:, 2, :], negr[:, :], negp[:, 1, :], ALU.subtract).then_inc(neg_split, 1)

            over_batches(pool, emit)

        @block.scalar
        def _(act):
            act.wait_ge(w_loaded, 64)
            act.activation(tokw[0][:, :, :], tok_stage, ACT.Copy).then_inc(w_top, 1)
            act.activation(qkvw[0][:, :, :], qkv_stage, ACT.Copy).then_inc(w_top, 1)
            act.wait_ge(w_split, 2)

            def emit(events, b, a):
                for kind, n in events:
                    if kind == "st":
                        g, k = divmod(n, NST)
                        j, h, q0, w = ST[k][0]
                        act.wait_ge(st_full, b * (NG * NST) + n + 1)
                        order = PV_ORDER.index(5 if j == 3 else j)
                        if later(b * (NG * NT) + (g - 1) * NT + order + 1):
                            act.wait_ge(pv_full, b * (NG * NT) + (g - 1) * NT + order + 1)
                        src = stb[n % STB][0:TT, 0:sum(c[3] for c in ST[k])]
                        if j == 4:
                            src = src.rearrange("p (h c) -> p h c", h=2)
                            dst = prob[4][:, h:h + 2, :]
                        elif j == 3:
                            dst = prob35[:, h, :]
                        else:
                            dst = prob[j][0:TT, h, q0 - TT * j:q0 - TT * j + w]
                        act.activation(dst, src, ACT.Exp, scale=DH ** -0.5).then_inc(exp_done, 1)
                    if kind == "v":
                        act.wait_ge(v_full, b * NT + n + 1)
                        if n == 0 and later(b):
                            act.wait_ge(pv_full, b * (NG * NT))
                        act.activation(vaug[:, n, :, 0:DH], pab[0:TT, 0:D].rearrange("p (h r) -> p h r", r=DH),
                                       ACT.Copy).then_inc(v_evac, 1)
                    if kind == "turn":
                        act.wait_ge(turn_full, a * 4 + n + 1)
                        c, half = n % 2, n // 2
                        act.activation(xnT[0][:, c, half * HALF:(half + 1) * HALF], pab[:, 0:HALF], ACT.Copy).then_inc(turn_top, 1)
                    if kind == "qk":
                        act.wait_ge(qk_full, a * 8 + n + 1)
                        if later(a * 8 + n - 1):
                            act.wait_ge(parts_stored[n % 2], a * (4 * 16 * NPART) + 16 * NPART * (n // 2))
                        act.activation(parts[:, n % 2, 0, :], pab[:, 0:HALF], ACT.Copy).then_inc(qk_top, 1)

            over_batches(act, emit)

        @block.vector
        def _(dve):
            dve.memset(mxp[:, :, :, :], -3.0e38)
            dve.wait_ge(w_top, 2)
            dve.tensor_tensor(tokw[1][:, :, :], tok_stage, tokw[0][:, :, :].bitcast(fp32), ALU.subtract).then_inc(w_split, 1)
            dve.tensor_tensor(qkvw[1][:, :, :], qkv_stage, qkvw[0][:, :, :].bitcast(fp32), ALU.subtract).then_inc(w_split, 1)
            dve.wait_ge(rows_loaded, 16 * 6)

            def emit(events, b, a):
                for kind, n in events:
                    if kind == "tok":
                        dve.wait_ge(tok_full, a * NT + n + 1)
                        if n == 0 and later(a):
                            dve.wait_ge(h1_stored, a * 16)
                        dve.tensor_tensor(h1[:, n, :], pab[0:TT, 0:D], tokb_row[:, :], ALU.add).then_inc(tok_evac, 1)
                        dve.wait_ge(tok_evac, a * NT + n + 1)
                        dve.bn_stats(stats[:, n, :], h1[:, n, :]).then_inc(bn_done, 1)
                        if n == NT - 1:
                            wait_apart(dve, bn_done, a * NT + NT, apart["dve"])
                            for i in range(NT):
                                dve.bn_aggr(mv[:, i, :], stats[:, i, :]).then_inc(aggr_done, 1)
                            dve.wait_ge(aggr_done, a * NT + NT)
                            dve.tensor_scalar(veps[:, :], mv[:, :, 1], EPS, None, ALU.add).then_inc(veps_ready, 1)
                    if kind == "norm_scale":
                        dve.wait_ge(rstd_ready, a + 1)
                        if later(a):
                            dve.wait_ge(turn_full, a * 4)
                        for i in range(NT):
                            dve.tensor_scalar(xn[:, i, :], h1[:, i, :], mv[:, i, 0:1], rstd[:, i:i + 1],
                                              ALU.subtract, ALU.mult).then_inc(xn_ready, 1)
                    if kind == "turn":
                        dve.wait_ge(turn_top, a * 4 + n + 1)
                        c, half = n % 2, n // 2
                        dve.tensor_tensor(xnT[1][:, c, half * HALF:(half + 1) * HALF], pab[:, 0:HALF],
                                          xnT[0][:, c, half * HALF:(half + 1) * HALF].bitcast(fp32),
                                          ALU.subtract).then_inc(turn_evac, 1)
                    if kind == "qk":
                        dve.wait_ge(qk_top, a * 8 + n + 1)
                        if later(a * 8 + n - 1):
                            dve.wait_ge(qk_low, a * 8 + n - 1)
                        dve.tensor_tensor(rest[:, n % 2, :], pab[:, 0:HALF], parts[:, n % 2, 0, :],
                                          ALU.subtract).then_inc(qk_evac, 1)
                    if kind == "mx":
                        i, h, heads, k0, w = MX[n % NMX]
                        dve.wait_ge(mx_full, b * (NG * NMX) + n + 1)
                        src = mxb[n % MXB][0:TT, 0:heads * w].rearrange("p (h c) -> p h c", h=heads)
                        slot = 1 if k0 else 0
                        dve.tensor_reduce(mxp[:, n // NMX % 2, h * NT + i:(h + heads - 1) * NT + i + 1:NT, slot], src,
                                          AX.X, ALU.max).then_inc(mx_red, 1)
                    if kind == "mx_row":
                        dve.wait_ge(mx_red, b * (NG * NMX) + (n + 1) * NMX)
                        if later(b * NG + n):
                            dve.wait_ge(max_full, b * NG + n)
                        dve.tensor_reduce(mxg[:, :], mxp[:, n % 2, :, :], AX.X, ALU.max).then_inc(row_max, 1)
                    if kind == "mx_neg":
                        dve.wait_ge(max_full, b * NG + n + 1)
                        if later(b * NG + n):
                            dve.wait_ge(neg_split, b * (4 * NG) + 4 * n)
                        dve.tensor_scalar(negm[:, :], pab[0:HG * NT, 0:TT], -1.0, None, ALU.mult).then_inc(max_evac, 1)
                    if kind == "attn_norm":
                        wait_apart(dve, pv_full, b * (NG * NT) + (n + 1) * NT, apart["dve"])
                        dve.stream_shuffle(sums[:, :].rearrange("p (s c) -> p s c", s=2), pvb[:, :, 0:HALF],
                                           [DH + r % DH for r in range(2 * DH)]).then_inc(sums_moved, 1)
                        dve.wait_ge(sums_moved, b * NG + n + 1)
                        dve.reciprocal(sums[:, :], sums[:, :]).then_inc(sums_inv, 1)
                        dve.wait_ge(sums_inv, b * NG + n + 1)
                        if n == 0 and later(b):
                            dve.wait_ge(proj_full, b * NT)
                        dve.tensor_tensor(onT[:, n, :].rearrange("p (s c) -> p s c", s=2), pvb[:, :, 0:HALF],
                                          sums[:, :].rearrange("p (s c) -> p s c", s=2), ALU.mult).then_inc(attn_evac, 1)
                    if kind == "proj":
                        dve.wait_ge(proj_full, b * NT + (n + 1 - NT))
                        if n == 0:
                            dve.wait_ge(res_loaded, b * 16)
                        dve.tensor_tensor(res[:, n, :], pab[0:TT, 0:D], res[:, n, :], ALU.add).then_inc(proj_evac, 1)

            over_batches(dve, emit)

        @block.tensor
        def _(pe):
            pe.wait_ge(consts, 9 + NG)
            pe.wait_ge(zeroed, 2)
            pe.wait_ge(w_split, 2)
            bank = {"by": None}

            def take_bank(kind, by, value):
                if bank["by"] is not None:
                    pe.wait_ge(*bank["by"])
                bank["by"] = (by, value)

            def split_product(out, lhs, rhs):
                steps = [(c, x, w) for c in range(len(lhs[0])) for x, w in ((0, 0), (0, 1), (1, 0))]
                for n, (c, x, w) in enumerate(steps):
                    done = nc.tensor.matmul(out, lhs[x][c], rhs[w][c], start=(n == 0), stop=(n == len(steps) - 1))
                return done

            def emit(events, b, a):
                events = list(events)
                if events[0][0] == "mx":
                    bank["by"] = (max_evac, b * NG + 1)
                for kind, n in events:
                    if kind == "tok":
                        if n == 0:
                            pe.wait_ge(x_split, a * KC + KC)
                        take_bank("tok", tok_evac, a * NT + n + 1)
                        split_product(pab[0:TT, 0:D],
                                      [[xp[p][:, c, TT * n + o:TT * n + o + TT] for o in SHIFTS for c in range(KC)] for p in range(2)],
                                      [[tokw[p][:, c, :] for c in range(3 * KC)] for p in range(2)]).then_inc(tok_full, 1)
                    if kind == "turn":
                        c, half = n % 2, n // 2
                        pe.wait_ge(xn_ready, a * NT + 3 * half + 3)
                        take_bank("turn", turn_evac, a * 4 + n + 1)
                        for i in range(3):
                            done = nc.tensor.transpose(pab[:, TT * i:TT * i + TT], xn[:, 3 * half + i, 128 * c:128 * c + 128],
                                                       ident[0:TT, 0:TT])
                        done.then_inc(turn_full, 1)
                    if kind == "qk":
                        m, which, half = n // 4, n // 2 % 2, n % 2
                        pe.wait_ge(turn_evac, a * 4 + 2 * half + 2)
                        take_bank("qk", qk_evac, a * 8 + n + 1)
                        split_product(pab[:, 0:HALF],
                                      [[qkvw[p][:, KC * which + c, 128 * m:128 * m + 128] for c in range(KC)] for p in range(2)],
                                      [[xnT[p][:, c, half * HALF:(half + 1) * HALF] for c in range(KC)] for p in range(2)]
                                      ).then_inc(qk_full, 1)
                    if kind == "v":
                        pe.wait_ge(turn_evac, b * 4 + 4)
                        take_bank("v", v_evac, b * NT + n + 1)
                        split_product(pab[0:TT, 0:D],
                                      [[xnT[p][:, c, TT * n:TT * n + TT] for c in range(KC)] for p in range(2)],
                                      [[qkvw[p][:, 2 * KC + c, :] for c in range(KC)] for p in range(2)]).then_inc(v_full, 1)
                    if kind == "proj":
                        if n == 0:
                            pe.wait_ge(attn_evac, b * NG)
                        take_bank("proj", proj_evac, b * NT + (n + 1 - NT))
                        for g in range(NG):
                            done = nc.tensor.matmul(pab[0:TT, 0:D], onT[:, g, TT * n:TT * n + TT], projw[:, g, :],
                                                    start=(g == 0), stop=(g == NG - 1))
                        done.then_inc(proj_full, 1)
                    if kind == "mx":
                        g, k = divmod(n, NMX)
                        i, h, heads, k0, w = MX[k]
                        if k == 0:
                            pe.wait_ge(stack_loaded[g % NG], b * (16 * 9) + 16 * 9 * (g // NG + 1))
                        if later(b * (NG * NMX) + n + 1 - MXB):
                            pe.wait_ge(mx_red, b * (NG * NMX) + n + 1 - MXB)
                        for e in range(heads):
                            out = mxb[n % MXB][0:TT, e * w:(e + 1) * w]
                            diag = k0 + w == (i + 1) * TT
                            done = nc.tensor.matmul(out, qst[g % NG][0:ROWS, h + e, TT * i:TT * i + TT],
                                                    kst[g % NG][0:ROWS, h + e, k0:k0 + w], start=True, stop=not diag)
                            if diag:
                                done = nc.tensor.matmul(out[:, w - TT:w], identb[:, :], mask_qk[:, :], start=False, stop=True)
                        done.then_inc(mx_full, 1)
                    if kind == "mx_turn":
                        pe.wait_ge(row_max, b * NG + n + 1)
                        take_bank("max", max_evac, b * NG + n + 1)
                        nc.tensor.transpose(pab[0:HG * NT, 0:TT], mxg[:, :], ident[0:TT, 0:TT]).then_inc(max_full, 1)
                    if kind == "st":
                        g, k = divmod(n, NST)
                        if k == 0:
                            pe.wait_ge(negm_loaded, b * (48 * NG) + 48 * (g + 1))
                        if later(b * (NG * NST) + n + 1 - STB):
                            pe.wait_ge(exp_done, b * (NG * NST) + n + 1 - STB)
                        at = 0
                        for j, h, q0, w in ST[k]:
                            out = stb[n % STB][0:TT, at:at + w]
                            diag = q0 == TT * j
                            done = nc.tensor.matmul(out, kst[g][:, h, TT * j:TT * j + TT], qst[g][:, h, q0:q0 + w],
                                                    start=True, stop=not diag)
                            if diag:
                                done = nc.tensor.matmul(out[:, 0:TT], identb[:, :], mask_kq[:, :], start=False, stop=True)
                            at += w
                        done.then_inc(st_full, 1)
                    if kind == "pv":
                        g, o = n
                        j = PV_ORDER[o]
                        pe.wait_ge(exp_done, b * (NG * NST) + g * NST + PV_AFTER[o])
                        if o == 0:
                            if g == 0:
                                pe.wait_ge(v_evac, b * NT + NT)
                            if later(b * NG + g):
                                pe.wait_ge(attn_evac, b * NG + g)
                        for s in range(2):
                            q0, q1 = max(TT * j, s * HALF), (s + 1) * HALF
                            if q0 >= q1:
                                continue
                            for h in range(HG):
                                if j in prob:
                                    p = prob[j][0:TT, h, q0 - TT * j:q1 - TT * j]
                                else:
                                    p = prob35[:, h, 0:3 * TT] if j == 3 else prob35[:, h, 3 * TT:4 * TT]
                                done = nc.tensor.matmul(pvb[2 * DH * h:2 * DH * (h + 1), s, q0 - s * HALF:q1 - s * HALF],
                                                        vaug[:, j, HG * g + h, :], p, start=(j == 0),
                                                        stop=(j == (2 if s == 0 else 4)))
                        done.then_inc(pv_full, 1)

            over_batches(pe, emit)
NE, H = 4, 1024
NM = H // 128
NCH = NE * NM
TOP = 2
HT = NT // 2
NHB = 2 * NB
BEHIND = 2
L1B, HFB, HPB = 4, 4, 4
GATE_STEPS = 10


def route_events():
    return (("load", 0), ("stats", 0), ("scale", 0), ("turn", 0), ("turn", 1), ("router", 0), ("gates", 0))


def expert_events(first, last):
    at = dict(zip((3, 4, 8, 12, 14, 18, 20), () if last else route_events()))
    for s in range(NCH):
        yield "l1", s
        if s >= BEHIND or not first:
            yield "l2", s - BEHIND
            if (s - BEHIND) % NM == NM - 1:
                yield "y", (s - BEHIND) // NM
        if s in at:
            yield at[s]


def last_events():
    for s in range(BEHIND):
        yield "l2", s - BEHIND
    yield "y", -1


def over_half_batches(eng, emit):
    emit(route_events(), -1, 1, -1)
    emit(expert_events(True, False), 0, 0, 0)
    emit(expert_events(False, False), 1, 1, 0)
    with eng.Fori(1, NB - 1) as b:
        emit(expert_events(False, False), b * 2, 0, b)
        emit(expert_events(False, False), b * 2 + 1, 1, b)
    emit(expert_events(False, False), NHB - 2, 0, NB - 1)
    emit(expert_events(False, True), NHB - 1, 1, NB - 1)
    emit(last_events(), NHB, 0, NB)


def expert_phase(nc, h2_s, w1, b1T, w2, b2, wr, br, out):
    with ExitStack() as es:
        def sb(name, shape, dt=fp32):
            return es.enter_context(nc.sbuf_tensor(name, shape, dt))

        def ps(name, shape):
            return es.enter_context(nc.psum_tensor(name, shape, fp32))

        def sem(name):
            return es.enter_context(nc.semaphore(name))

        w1p = [sb(f"w1p{p}", [128, NE, KC, H], fp32r) for p in range(2)]
        w2p = [sb(f"w2p{p}", [128, NE, NM, D], fp32r) for p in range(2)]
        wrp = [sb(f"wrp{p}", [128, KC, NE], fp32r) for p in range(2)]
        stage = sb("stage", [128, 2, KC * H])
        wr_raw = sb("wr_raw", [128, KC, NE])
        b1c = sb("b1c", [128, NCH])
        gb1 = sb("gb1", [128, NCH])
        gb1p = [sb(f"gb1p{p}", [128, NCH], fp32r) for p in range(2)]
        b2row = sb("b2row", [1, NE, D])
        crow = sb("crow", [1, NE, D])
        csum = sb("csum", [1, D])
        drow = sb("drow", [1, NE, D])
        dall = sb("dall", [TT, NE, D])
        ones = sb("ones", [1, TT])
        br_row = sb("br_row", [TT, NE])
        before = sb("before", [TT, NE, NE])
        ident2 = sb("ident2", [128, 128])
        power2 = sb("power2", [TT, HT])
        h2t = sb("h2t", [TT, 2, HT, D])
        stats2 = sb("stats2", [TT, HT, 6])
        mv2 = sb("mv2", [TT, HT, 2])
        veps2 = sb("veps2", [TT, HT])
        rstd2 = sb("rstd2", [TT, HT])
        xn2 = sb("xn2", [TT, HT, D])
        x2T = [sb(f"x2T{p}", [128, 2, KC, HALF], fp32r) for p in range(2)]
        logit = sb("logit", [TT, HT, NE])
        above = sb("above", [TT, HT, NE, NE])
        level = sb("level", [TT, HT, NE, NE])
        rank = sb("rank", [TT, HT, NE])
        chosen = sb("chosen", [TT, HT, NE])
        picked = sb("picked", [TT, HT, NE])
        total = sb("total", [TT, HT])
        margin = sb("margin", [TT, HT, NE])
        tanh = sb("tanh", [TT, HT, NE])
        gate = sb("gate", [TT, 2, HT, NE])
        hf = sb("hf", [128, HFB, HALF])
        hp = [sb(f"hp{p}", [128, HPB, HALF], fp32r) for p in range(2)]

        l1b = [ps(f"l1b{i}", [128, 512]) for i in range(L1B)]
        yb = [ps(f"yb{i}", [128, 512]) for i in range(HT)]
        rb = ps("rb", [128, 512])

        w_loaded = [sem(f"w_loaded_{i}") for i in range(2)]
        wt_top, wt_split, small_loaded, consts2 = sem("wt_top"), sem("wt_split"), sem("small_loaded"), sem("consts2")
        gb_ready, gb_top, gb_split, c_full, c_sum, d_full, d_ready = (sem(n) for n in (
            "gb_ready", "gb_top", "gb_split", "c_full", "c_sum", "d_full", "d_ready"))
        h2_loaded = [sem(f"h2_loaded{i}") for i in range(2)]
        bn2_done, aggr2_done, veps2_ready, rstd2_ready, xn2_ready = (sem(n) for n in (
            "bn2_done", "aggr2_done", "veps2_ready", "rstd2_ready", "xn2_ready"))
        turn2_full, turn2_top, turn2_evac, router_full = (sem(n) for n in (
            "turn2_full", "turn2_top", "turn2_evac", "router_full"))
        gate_step, tanh_ready, gate_ready = sem("gate_step"), sem("tanh_ready"), sem("gate_ready")
        l1_full, gelu_done, h_top, h_split, l2_full = (sem(n) for n in (
            "l1_full", "gelu_done", "h_top", "h_split", "l2_full"))
        y_full, y_evac, acc_ready = sem("y_full"), sem("y_evac"), sem("acc_ready")
        out_stored = [sem(f"out_stored{i}") for i in range(2)]
        apart = {e: sem(f"apart2_{e}") for e in ("sp", "act", "dve")}
        block = es.enter_context(nc.Block())

        def tokens(t, b, half):
            return t[b, half * HALF:(half + 1) * HALF, :].rearrange("(i p) d -> p i d", p=TT)

        BLOCKS = [(e, k) for e in range(NE) for k in range(2)]

        def split_dst(p, e, k):
            return (w2p if k else w1p)[p][:, e, :, :].rearrange("p c d -> p (c d)")

        @block.sync
        def _(sp):
            sp.dma_start(wr_raw[:, :, :], wr.rearrange("(c p) e -> p c e", p=128)).then_inc(small_loaded, 16)
            sp.dma_start(b1c[:, :], b1T).then_inc(small_loaded, 16)
            sp.dma_start(b2row[:, :, :], b2.rearrange("(a e) d -> a e d", a=1)).then_inc(small_loaded, 16)
            sp.dma_start(br_row[:, :], br.partition_broadcast(TT)).then_inc(small_loaded, 16)
            for n, (e, k) in enumerate(BLOCKS):
                src = (w2[e] if k else w1[e]).rearrange("(c p) d -> p c d", p=128)
                if n >= 2:
                    sp.wait_ge(wt_split, n - 1)
                sp.dma_start(stage[:, n % 2, :].rearrange("p (c d) -> p c d", d=src.shape[2]), src).then_inc(w_loaded[n % 2], 16)

            def emit(events, g, side, b):
                for kind, n in events:
                    if kind == "load":
                        nb, half = (b + 1, 0) if side else (b, 1)
                        if later(g * 8 + 8 * side):
                            wait_apart(sp, out_stored[1 - side], g * 8 + 8 * side, apart["sp"])
                        sp.dma_start(h2t[:, 1 - side, :, :], tokens(h2_s, nb, half)).then_inc(h2_loaded[1 - side], 16)
                    if kind == "y" and n == -1:
                        wait_apart(sp, y_evac, g * (NE * HT), apart["sp"])
                        nb, half = (b, 0) if side else (b - 1, 1)
                        sp.dma_start(tokens(out, nb, half), h2t[:, 1 - side, :, :]).then_inc(out_stored[1 - side], 16)

            over_half_batches(sp, emit)
            for i in range(2):
                sp.wait_ge(out_stored[i], NB * 16)

        @block.gpsimd
        def _(pool):
            pool.memset(ident2[:, :], 0.0).then_inc(consts2, 1)
            pool.memset(power2[:, :], -0.5).then_inc(consts2, 1)
            pool.memset(before[:, :, :], 1.0).then_inc(consts2, 1)
            pool.memset(ones[:, :], 1.0).then_inc(consts2, 1)
            pool.wait_ge(consts2, 4)
            pool.affine_select(out=ident2[:, :], in_=ident2[:, :], compare_op=ALU.not_equal, fill=1.0, base=0,
                               pattern=[[-1, 128]], channel_multiplier=1).then_inc(consts2, 1)
            pool.affine_select(out=before[:, :, :], in_=before[:, :, :], compare_op=ALU.is_gt, fill=0.0, base=0,
                               pattern=[[1, NE], [-1, NE]], channel_multiplier=0).then_inc(consts2, 1)

            def emit(events, g, side, b):
                for kind, n in events:
                    if kind == "scale":
                        pool.wait_ge(veps2_ready, g + 2)
                        pool.tensor_tensor(rstd2[:, :], veps2[:, :], power2[:, :], ALU.pow).then_inc(rstd2_ready, 1)

            over_half_batches(pool, emit)

        @block.scalar
        def _(act):
            act.wait_ge(small_loaded, 64)
            act.activation(gb1[:, :], b1c[:, :], ACT.Gelu).then_inc(gb_ready, 1)
            for n, (e, k) in enumerate(BLOCKS):
                act.wait_ge(w_loaded[n % 2], 16 * (n // 2 + 1))
                act.activation(split_dst(0, e, k), stage[:, n % 2, :], ACT.Copy).then_inc(wt_top, 1)

            def emit(events, g, side, b):
                for kind, n in events:
                    if kind == "l1":
                        act.wait_ge(l1_full, g * NCH + n + 1)
                        if later(g * NCH + n + 1 - HFB):
                            act.wait_ge(h_split, g * NCH + n + 1 - HFB)
                        act.activation(hf[:, n % HFB, :], l1b[n % L1B][:, 0:HALF], ACT.Gelu,
                                       bias=b1c[:, n:n + 1]).then_inc(gelu_done, 1)
                    if kind == "turn":
                        act.wait_ge(turn2_full, g * KC + KC + n + 1)
                        act.activation(x2T[0][:, 1 - side, n, :], rb[:, 0:HALF], ACT.Copy).then_inc(turn2_top, 1)
                    if kind == "gates":
                        act.wait_ge(gate_step, g * GATE_STEPS + 2 * GATE_STEPS)
                        act.activation(tanh[:, :, :], margin[:, :, :], ACT.Tanh, scale=0.5).then_inc(tanh_ready, 1)

            over_half_batches(act, emit)

        @block.vector
        def _(dve):
            dve.wait_ge(small_loaded, 64)
            dve.tensor_copy(wrp[0][:, :, :], wr_raw[:, :, :]).then_inc(gb_top, 1)
            dve.wait_ge(gb_ready, 1)
            dve.tensor_copy(gb1p[0][:, :], gb1[:, :]).then_inc(gb_top, 1)
            dve.wait_ge(gb_top, 2)
            dve.tensor_tensor(wrp[1][:, :, :], wr_raw[:, :, :], wrp[0][:, :, :].bitcast(fp32), ALU.subtract).then_inc(gb_split, 1)
            dve.tensor_tensor(gb1p[1][:, :], gb1[:, :], gb1p[0][:, :].bitcast(fp32), ALU.subtract).then_inc(gb_split, 1)
            for n, (e, k) in enumerate(BLOCKS):
                dve.wait_ge(wt_top, n + 1)
                dve.tensor_tensor(split_dst(1, e, k), stage[:, n % 2, :], split_dst(0, e, k).bitcast(fp32),
                                  ALU.subtract).then_inc(wt_split, 1)
            dve.wait_ge(c_full, NE)
            for e in range(NE):
                dve.tensor_tensor(crow[:, e, :], yb[e // 2][0:1, D * (e % 2):D * (e % 2) + D], b2row[:, e, :], ALU.add).then_inc(c_sum, 1)
            dve.wait_ge(c_sum, NE)
            dve.tensor_tensor(csum[:, :], crow[:, 0, :], crow[:, 1, :], ALU.add).then_inc(c_sum, 1)
            for e in range(2, NE):
                dve.wait_ge(c_sum, NE + e - 1)
                dve.tensor_tensor(csum[:, :], csum[:, :], crow[:, e, :], ALU.add).then_inc(c_sum, 1)
            dve.tensor_tensor(drow[:, :, :], b2row[:, :, :], crow[:, :, :], ALU.subtract).then_inc(c_sum, 1)
            dve.wait_ge(c_sum, 2 * NE)
            for e in range(NE):
                dve.tensor_tensor(drow[:, e, :], drow[:, e, :], csum[:, :], ALU.add).then_inc(c_sum, 1)
            dve.wait_ge(d_full, NE)
            for e in range(NE):
                dve.tensor_copy(dall[:, e, :], yb[e // 2][0:TT, D * (e % 2):D * (e % 2) + D]).then_inc(d_ready, 1)
            dve.wait_ge(consts2, 6)

            def emit(events, g, side, b):
                for kind, n in events:
                    other = 1 - side
                    if kind == "stats":
                        dve.wait_ge(h2_loaded[other], g * 8 + 8 * side + 16)
                        for i in range(HT):
                            dve.bn_stats(stats2[:, i, :], h2t[:, other, i, :]).then_inc(bn2_done, 1)
                        wait_apart(dve, bn2_done, g * HT + 2 * HT, apart["dve"])
                        for i in range(HT):
                            dve.bn_aggr(mv2[:, i, :], stats2[:, i, :]).then_inc(aggr2_done, 1)
                        dve.wait_ge(aggr2_done, g * HT + 2 * HT)
                        dve.tensor_scalar(veps2[:, :], mv2[:, :, 1], EPS, None, ALU.add).then_inc(veps2_ready, 1)
                    if kind == "scale":
                        dve.wait_ge(rstd2_ready, g + 2)
                        if later(g + 1):
                            dve.wait_ge(turn2_full, g * KC + KC)
                        for i in range(HT):
                            dve.tensor_scalar(xn2[:, i, :], h2t[:, other, i, :], mv2[:, i, 0:1], rstd2[:, i:i + 1],
                                              ALU.subtract, ALU.mult).then_inc(xn2_ready, 1)
                    if kind == "turn":
                        dve.wait_ge(turn2_top, g * KC + KC + n + 1)
                        dve.tensor_tensor(x2T[1][:, other, n, :], rb[:, 0:HALF], x2T[0][:, other, n, :].bitcast(fp32),
                                          ALU.subtract).then_inc(turn2_evac, 1)
                    if kind == "router":
                        steps = g * GATE_STEPS + GATE_STEPS
                        dve.wait_ge(router_full, g + 2)
                        dve.tensor_tensor(logit[:, :, :], rb[0:TT, 0:HT * NE].rearrange("p (i e) -> p i e", e=NE),
                                          br_row[:, :].unsqueeze(1).broadcast_to([TT, HT, NE]), ALU.add).then_inc(gate_step, 1)
                        dve.wait_ge(gate_step, steps + 1)
                        shape = [TT, HT, NE, NE]
                        own, rival = logit[:, :, :].unsqueeze(3).broadcast_to(shape), logit[:, :, :].unsqueeze(2).broadcast_to(shape)
                        dve.tensor_tensor(above[:, :, :, :], rival, own, ALU.is_gt).then_inc(gate_step, 1)
                        dve.tensor_tensor(level[:, :, :, :], rival, own, ALU.is_equal).then_inc(gate_step, 1)
                        dve.wait_ge(gate_step, steps + 3)
                        dve.tensor_tensor(level[:, :, :, :], level[:, :, :, :], before[:, :, :].unsqueeze(1).broadcast_to(shape),
                                          ALU.mult).then_inc(gate_step, 1)
                        dve.wait_ge(gate_step, steps + 4)
                        dve.tensor_tensor(above[:, :, :, :], above[:, :, :, :], level[:, :, :, :], ALU.add).then_inc(gate_step, 1)
                        dve.wait_ge(gate_step, steps + 5)
                        dve.tensor_reduce(rank[:, :, :], above[:, :, :, :], AX.X, ALU.add).then_inc(gate_step, 1)
                        dve.wait_ge(gate_step, steps + 6)
                        dve.tensor_scalar(chosen[:, :, :], rank[:, :, :], TOP - 0.5, None, ALU.is_lt).then_inc(gate_step, 1)
                        dve.wait_ge(gate_step, steps + 7)
                        dve.tensor_tensor(picked[:, :, :], chosen[:, :, :], logit[:, :, :], ALU.mult).then_inc(gate_step, 1)
                        dve.wait_ge(gate_step, steps + 8)
                        dve.tensor_reduce(total[:, :], picked[:, :, :], AX.X, ALU.add).then_inc(gate_step, 1)
                        dve.wait_ge(gate_step, steps + 9)
                        dve.scalar_tensor_tensor(margin[:, :, :], logit[:, :, :], 2.0,
                                                 total[:, :].unsqueeze(2).broadcast_to([TT, HT, NE]),
                                                 ALU.mult, ALU.subtract).then_inc(gate_step, 1)
                    if kind == "gates":
                        dve.wait_ge(tanh_ready, g + 2)
                        dve.tensor_scalar(tanh[:, :, :], tanh[:, :, :], 0.5, 0.5, ALU.mult, ALU.add).then_inc(gate_ready, 1)
                        dve.wait_ge(gate_ready, g * 2 + 3)
                        dve.tensor_tensor(gate[:, other, :, :], tanh[:, :, :], chosen[:, :, :], ALU.mult).then_inc(gate_ready, 1)
                        dve.wait_ge(gate_ready, g * 2 + 4)
                        for e in range(NE):
                            for i in range(HT):
                                dve.scalar_tensor_tensor(h2t[:, other, i, :], dall[:, e, :], gate[:, other, i, e:e + 1],
                                                         h2t[:, other, i, :], ALU.mult, ALU.add).then_inc(acc_ready, 1)
                            dve.wait_ge(acc_ready, g * (NE * HT) + NE * HT + (e + 1) * HT)
                    if kind == "l1":
                        if later(g * NCH + n + 1 - HPB):
                            dve.wait_ge(l2_full, g * NCH + n + 1 - HPB)
                        dve.wait_ge(gelu_done, g * NCH + n + 1)
                        dve.tensor_copy(hp[0][:, n % HPB, :], hf[:, n % HFB, :]).then_inc(h_top, 1)
                        dve.wait_ge(h_top, g * NCH + n + 1)
                        dve.tensor_tensor(hp[1][:, n % HPB, :], hf[:, n % HFB, :], hp[0][:, n % HPB, :].bitcast(fp32),
                                          ALU.subtract).then_inc(h_split, 1)
                    if kind == "y":
                        at, e = (other, NE - 1) if n < 0 else (side, n)
                        if later(g * (NE * HT) + n * HT):
                            dve.wait_ge(y_evac, g * (NE * HT) + n * HT)
                        for i in range(HT):
                            if i < HT - 1:
                                dve.wait_ge(y_full, g * (NE * (HT - 1)) + n * (HT - 1) + i + 1)
                            else:
                                dve.wait_ge(l2_full, g * NCH + (n + 1) * NM)
                            dve.scalar_tensor_tensor(h2t[:, at, i, :], yb[i][0:TT, 0:D], gate[:, at, i, e:e + 1],
                                                     h2t[:, at, i, :], ALU.mult, ALU.add).then_inc(y_evac, 1)

            over_half_batches(dve, emit)

        @block.tensor
        def _(pe):
            pe.wait_ge(consts2, 6)
            pe.wait_ge(gb_split, 2)
            pe.wait_ge(wt_split, 2 * NE)
            for e in range(NE):
                for m in range(NM):
                    col = slice(NM * e + m, NM * e + m + 1)
                    for x, w in ((0, 0), (0, 1), (1, 0)):
                        done = nc.tensor.matmul(yb[e // 2][0:1, D * (e % 2):D * (e % 2) + D], gb1p[x][:, col], w2p[w][:, e, m, :],
                                                start=(m == 0 and (x, w) == (0, 0)), stop=(m == NM - 1 and x == 1))
                done.then_inc(c_full, 1)
            pe.wait_ge(c_sum, 3 * NE)
            for e in range(NE):
                nc.tensor.matmul(yb[e // 2][0:TT, D * (e % 2):D * (e % 2) + D], ones[:, :], drow[:, e, :],
                                 start=True, stop=True).then_inc(d_full, 1)
            pe.wait_ge(d_ready, NE)

            def emit(events, g, side, b):
                other = 1 - side
                for kind, n in events:
                    if kind == "turn":
                        pe.wait_ge(xn2_ready, g * HT + 2 * HT)
                        if n:
                            pe.wait_ge(turn2_evac, g * KC + KC + n)
                        elif later(g + 1):
                            pe.wait_ge(gate_step, g * GATE_STEPS + 1)
                        for i in range(HT):
                            done = nc.tensor.transpose(rb[:, TT * i:TT * i + TT], xn2[:, i, 128 * n:128 * n + 128],
                                                       ident2[0:TT, 0:TT])
                        done.then_inc(turn2_full, 1)
                    if kind == "router":
                        pe.wait_ge(turn2_evac, g * KC + 2 * KC)
                        for i in range(HT):
                            steps = [(c, x, w) for c in range(KC) for x, w in ((0, 0), (0, 1), (1, 0))]
                            for k, (c, x, w) in enumerate(steps):
                                done = nc.tensor.matmul(rb[0:TT, NE * i:NE * i + NE], x2T[x][:, other, c, TT * i:TT * i + TT],
                                                        wrp[w][:, c, :], start=(k == 0), stop=(k == len(steps) - 1))
                        done.then_inc(router_full, 1)
                    if kind == "l1":
                        e, m = divmod(n, NM)
                        if n == 0:
                            pe.wait_ge(turn2_evac, g * KC + KC)
                        if later(g * NCH + n + 1 - L1B):
                            pe.wait_ge(gelu_done, g * NCH + n + 1 - L1B)
                        steps = [(c, x, w) for c in range(KC) for w, x in ((0, 0), (0, 1), (1, 0))]
                        for k, (c, x, w) in enumerate(steps):
                            done = nc.tensor.matmul(l1b[n % L1B][:, 0:HALF], w1p[w][:, e, c, 128 * m:128 * m + 128],
                                                    x2T[x][:, side, c, :], start=(k == 0), stop=(k == len(steps) - 1))
                        done.then_inc(l1_full, 1)
                    if kind == "l2":
                        e, m = divmod(n % NCH, NM)
                        pe.wait_ge(h_split, g * NCH + n + 1)
                        for i in range(HT):
                            if m == 0 and later(g * (NE * HT) + (n // NM - 1) * HT + i + 1):
                                pe.wait_ge(y_evac, g * (NE * HT) + (n // NM - 1) * HT + i + 1)
                            for x, w in ((0, 0), (0, 1), (1, 0)):
                                done = nc.tensor.matmul(yb[i][0:TT, 0:D], hp[x][:, n % HPB, TT * i:TT * i + TT],
                                                        w2p[w][:, e, m, :], start=(m == 0 and (x, w) == (0, 0)),
                                                        stop=(m == NM - 1 and x == 1))
                            if m == NM - 1 and i < HT - 1:
                                done.then_inc(y_full, 1)
                        done.then_inc(l2_full, 1)

            over_half_batches(pe, emit)


def program(nc, x, tok_W, tok_b, Wk, Wq, Wv, Wp, bp, w1, b1, w2, b2, wr, br, out):
    h1_s = nc.dram_tensor("h1_s", [NB, T, D], fp32, kind="Internal").ap()
    qk_s = nc.dram_tensor("qk_s", [NB, 2, NH, NPART, DH, T], bf16, kind="Internal").ap()
    h2_s = nc.dram_tensor("h2_s", [NB, T, D], fp32, kind="Internal").ap()
    attention_phase(nc, x, tok_W, tok_b, Wk, Wq, Wv, Wp, bp, h1_s, qk_s, h2_s)
    expert_phase(nc, h2_s, w1, b1, w2, b2, wr, br, out)


def kernel(x, L0_tok_W, L0_tok_b, L0_attn_Wk, L0_attn_Wq, L0_attn_Wv, L0_attn_Wp, L0_attn_bp,
           L0_ffn_w1, L0_ffn_b1, L0_ffn_w2, L0_ffn_b2, L0_ffn_wr, L0_ffn_br):
    import concourse.bacc as bacc
    from concourse.bass_utils import run_bass_kernel_spmd

    laid = {
        "x_T": np.asarray(x).transpose(0, 2, 1), "tok_W_T": np.asarray(L0_tok_W).T, "tok_b": L0_tok_b,
        "Wk_T": np.asarray(L0_attn_Wk).T, "Wq_T": np.asarray(L0_attn_Wq).T, "Wv_T": np.asarray(L0_attn_Wv).T,
        "Wp_T": np.asarray(L0_attn_Wp).T, "bp": L0_attn_bp, "w1": L0_ffn_w1,
        "b1_T": np.asarray(L0_ffn_b1).reshape(NCH, 128).T, "w2": L0_ffn_w2, "b2": L0_ffn_b2,
        "wr": L0_ffn_wr, "br": L0_ffn_br,
    }
    arrays = {f"in_{name}": np.ascontiguousarray(a) for name, a in laid.items()}
    nc = bacc.Bacc("TRN2", target_bir_lowering=False, num_devices=1)
    args = [nc.dram_tensor(name, a.shape, mybir.dt.from_np(a.dtype), kind="ExternalInput").ap()
            for name, a in arrays.items()]
    out = nc.dram_tensor("out", (NB, T, D), fp32, kind="ExternalOutput").ap()
    program(nc, *args, out)
    return run_bass_kernel_spmd(nc, [arrays], core_ids=[0]).results[0]["out"]
```
